# Optimizing a Trainium2 kernel written in Bass

```python
import numpy as np
import jax
import jax.numpy as jnp

def _softmax(x, axis=-1):
    return jax.nn.softmax(x, axis=axis)

def _gelu(x):
    return jax.nn.gelu(x, approximate=True)

def _silu(x):
    return jax.nn.silu(x)

def _sigmoid(x):
    return jax.nn.sigmoid(x)

def _layernorm(x, axis=-1, eps=1e-05):
    m = jnp.mean(x, axis=axis, keepdims=True)
    v = jnp.var(x, axis=axis, keepdims=True)
    return (x - m) / jnp.sqrt(v + eps)

def _scatter_add(tgt, idx, src, axis=0):
    return tgt.at[idx].add(src)

def _segment_sum(src, seg, n):
    return jax.ops.segment_sum(src, seg, n)
kernel_name = 'mk_decoder_postln_d1_seqx_r4_e786a2'

def setup_inputs(seed: int=0):
    np.random.seed(seed)
    _w = jnp.asarray

    def _rec_inputs():
        import jax
        import jax.numpy as jnp
        _rk = jax.random.key(seed)
        x = -0.0003929 + 0.9999 * jax.random.normal(jax.random.fold_in(_rk, 1), (16, 256, 256), jnp.float32)
        _lenS = 256 - jax.random.randint(jax.random.fold_in(_rk, 7), (16,), 0, max(1, 256 // 4) + 1, jnp.int32)
        _lenS2 = 256 - jax.random.randint(jax.random.fold_in(_rk, 8), (16,), 0, max(1, 256 // 4) + 1, jnp.int32)
        _ctx_1024P = jax.random.normal(jax.random.fold_in(_rk, 11), (16, 16, 256), jnp.float32)
        _ctx_1024c = jax.random.dirichlet(jax.random.fold_in(_rk, 511), 0.3 * jnp.ones((16,), jnp.float32), (16, 256))
        _ctx_1024t = jnp.einsum('bsk,bkd->bsd', _ctx_1024c, _ctx_1024P)
        _ctx_1024t = _ctx_1024t * jax.lax.rsqrt(jnp.mean(jnp.square(_ctx_1024t)) + 1e-12) * 0.953939
        ctx_1024 = 2.81802e-05 + 1.00001 * (_ctx_1024t + 0.3 * jax.random.normal(jax.random.fold_in(_rk, 611), (16, 256, 256), jnp.float32))
        return (x, ctx_1024)
    x, ctx_1024 = _rec_inputs()

    def _L0_attn_setup():
        import jax, jax.numpy as jnp
        import numpy as np
        DIM = 256
        NHEAD = 16
        HEAD_DIM = DIM // NHEAD

        def _rotate_half(t):
            h = t.shape[-1] // 2
            return jnp.concatenate([-t[..., h:], t[..., :h]], axis=-1)
        key = jax.random.key(seed)
        ks = jax.random.split(key, 5)
        B, N = (4, 512)
        return {'x': jax.random.normal(ks[0], (B, N, DIM), dtype=jnp.float32), 'qkv_w': jax.random.normal(ks[1], (3 * DIM, DIM), dtype=jnp.float32) * 0.02, 'qkv_b': jax.random.normal(ks[2], (3 * DIM,), dtype=jnp.float32) * 0.02, 'proj_w': jax.random.normal(ks[3], (DIM, DIM), dtype=jnp.float32) * 0.02, 'proj_b': jax.random.normal(ks[4], (DIM,), dtype=jnp.float32) * 0.02}
    _L0_attn_all = _L0_attn_setup()
    _L0_attn_in = {k: v for k, v in _L0_attn_all.items() if k in ('qkv_w', 'qkv_b', 'proj_w', 'proj_b')}
    del _L0_attn_all

    def _L0_xattn_setup():
        import jax, jax.numpy as jnp
        import numpy as np
        DIM = 256
        B, SQ, SK = (8, 512, 512)
        key = jax.random.key(seed)
        ks = jax.random.split(key, 8)
        s = 1.0 / np.sqrt(DIM)
        return {'x': jax.random.normal(ks[0], (B, SQ, DIM), dtype=jnp.float32), 'context': jax.random.normal(ks[1], (B, SK, DIM), dtype=jnp.float32), 'Wq': jax.random.normal(ks[2], (DIM, DIM), dtype=jnp.float32) * s, 'bq': jnp.zeros((DIM,), dtype=jnp.float32), 'Wk': jax.random.normal(ks[3], (DIM, DIM), dtype=jnp.float32) * s, 'bk': jnp.zeros((DIM,), dtype=jnp.float32), 'Wv': jax.random.normal(ks[4], (DIM, DIM), dtype=jnp.float32) * s, 'bv': jnp.zeros((DIM,), dtype=jnp.float32)}
    _L0_xattn_all = _L0_xattn_setup()
    _L0_xattn_in = {k: v for k, v in _L0_xattn_all.items() if k in ('Wq', 'bq', 'Wk', 'bk', 'Wv', 'bv')}
    del _L0_xattn_all

    def _L0_ffn_setup():
        import jax, jax.numpy as jnp
        import numpy as np
        HIDDEN = 256
        MOE_FF = 128
        SHARED_FF = 704
        NUM_EXPERTS = 16
        TOP_K = 2
        NORM_TOPK = True
        key = jax.random.key(seed)
        ks = jax.random.split(key, 8)
        s = 0.02
        return {'layer_input': jax.random.normal(ks[0], (1, 512, HIDDEN), dtype=jnp.float32), 'gate_w': jax.random.normal(ks[1], (NUM_EXPERTS, HIDDEN), dtype=jnp.float32) * s, 'w_gate_up': jax.random.normal(ks[2], (NUM_EXPERTS, HIDDEN, 2 * MOE_FF), dtype=jnp.float32) * s, 'w_down': jax.random.normal(ks[3], (NUM_EXPERTS, MOE_FF, HIDDEN), dtype=jnp.float32) * s, 'shared_w_gate': jax.random.normal(ks[4], (SHARED_FF, HIDDEN), dtype=jnp.float32) * s, 'shared_w_up': jax.random.normal(ks[5], (SHARED_FF, HIDDEN), dtype=jnp.float32) * s, 'shared_w_down': jax.random.normal(ks[6], (HIDDEN, SHARED_FF), dtype=jnp.float32) * s, 'shared_gate_w': jax.random.normal(ks[7], (1, HIDDEN), dtype=jnp.float32) * s}
    _L0_ffn_all = _L0_ffn_setup()
    _L0_ffn_in = {k: v for k, v in _L0_ffn_all.items() if k in ('gate_w', 'w_gate_up', 'w_down', 'shared_w_gate', 'shared_w_up', 'shared_w_down', 'shared_gate_w')}
    del _L0_ffn_all
    return {'x': x, 'ctx_1024': ctx_1024, 'L0_attn_qkv_w': _L0_attn_in['qkv_w'], 'L0_attn_qkv_b': _L0_attn_in['qkv_b'], 'L0_attn_proj_w': _L0_attn_in['proj_w'], 'L0_attn_proj_b': _L0_attn_in['proj_b'], 'L0_xattn_Wq': _L0_xattn_in['Wq'], 'L0_xattn_bq': _L0_xattn_in['bq'], 'L0_xattn_Wk': _L0_xattn_in['Wk'], 'L0_xattn_bk': _L0_xattn_in['bk'], 'L0_xattn_Wv': _L0_xattn_in['Wv'], 'L0_xattn_bv': _L0_xattn_in['bv'], 'L0_ffn_gate_w': _L0_ffn_in['gate_w'], 'L0_ffn_w_gate_up': _L0_ffn_in['w_gate_up'], 'L0_ffn_w_down': _L0_ffn_in['w_down'], 'L0_ffn_shared_w_gate': _L0_ffn_in['shared_w_gate'], 'L0_ffn_shared_w_up': _L0_ffn_in['shared_w_up'], 'L0_ffn_shared_w_down': _L0_ffn_in['shared_w_down'], 'L0_ffn_shared_gate_w': _L0_ffn_in['shared_gate_w']}

def reference(x, ctx_1024, L0_attn_qkv_w, L0_attn_qkv_b, L0_attn_proj_w, L0_attn_proj_b, L0_xattn_Wq, L0_xattn_bq, L0_xattn_Wk, L0_xattn_bk, L0_xattn_Wv, L0_xattn_bv, L0_ffn_gate_w, L0_ffn_w_gate_up, L0_ffn_w_down, L0_ffn_shared_w_gate, L0_ffn_shared_w_up, L0_ffn_shared_w_down, L0_ffn_shared_gate_w):
    import jax
    import jax.numpy as jnp

    def _L0_attn_ref(x, qkv_w, qkv_b, proj_w, proj_b):
        import jax, jax.numpy as jnp
        import numpy as np
        DIM = 256
        NHEAD = 16
        HEAD_DIM = DIM // NHEAD

        def _rotate_half(t):
            h = t.shape[-1] // 2
            return jnp.concatenate([-t[..., h:], t[..., :h]], axis=-1)
        B, N, D = x.shape
        H, hd = (NHEAD, HEAD_DIM)
        qkv = x @ qkv_w.T + qkv_b
        qkv = jnp.transpose(qkv.reshape(B, N, 3, H, hd), (2, 0, 3, 1, 4))
        q, k, v = (qkv[0], qkv[1], qkv[2])
        inv_freq = 1.0 / 10000.0 ** (jnp.arange(0, hd, 2, dtype=x.dtype) / hd)
        pos = jnp.arange(N, dtype=x.dtype)
        freqs = pos[:, None] * inv_freq[None, :]
        emb = jnp.concatenate([freqs, freqs], axis=-1)
        cos = jnp.cos(emb)[None, None, None]
        sin = jnp.sin(emb)[None, None, None]
        q = q * cos + _rotate_half(q) * sin
        k = k * cos + _rotate_half(k) * sin
        scale = hd ** (-0.5)
        attn = jnp.einsum('abhqd,abhkd->abhqk', q, k) * scale
        attn = jax.nn.softmax(attn, axis=-1)
        out = jnp.einsum('abhqk,bhkd->abhqd', attn, v)
        out = jnp.swapaxes(out, 1, 2).reshape(B, N, D)
        out = out @ proj_w.T + proj_b
        return out

    def _L0_xattn_ref(x, context, Wq, bq, Wk, bk, Wv, bv):
        import jax, jax.numpy as jnp
        import numpy as np
        DIM = 256
        B, SQ, SK = (8, 512, 512)
        q = jnp.einsum('bsd,ed->bse', x, Wq) + bq
        k = jnp.einsum('btd,ed->bte', context, Wk) + bk
        v = jnp.einsum('btd,ed->bte', context, Wv) + bv
        scale = 1.0 / jnp.sqrt(jnp.asarray(x.shape[-1], dtype=x.dtype))
        scores = jnp.einsum('bse,bte->bst', q, k) * scale
        attn = jax.nn.softmax(scores, axis=-1)
        return jnp.einsum('bst,bte->bse', attn, v)

    def _L0_ffn_ref(layer_input, gate_w, w_gate_up, w_down, shared_w_gate, shared_w_up, shared_w_down, shared_gate_w):
        import jax, jax.numpy as jnp
        import numpy as np
        HIDDEN = 256
        MOE_FF = 128
        SHARED_FF = 704
        NUM_EXPERTS = 16
        TOP_K = 2
        NORM_TOPK = True
        B, S, D = layer_input.shape
        x = layer_input.reshape(-1, D)
        N = x.shape[0]
        shared = jax.nn.silu(x @ shared_w_gate.T) * (x @ shared_w_up.T) @ shared_w_down.T
        shared = shared * jax.nn.sigmoid(x @ shared_gate_w.T)
        logits = x @ gate_w.T
        probs = jax.nn.softmax(logits.astype(jnp.float32), axis=-1)
        rw, sel = jax.lax.top_k(probs, TOP_K)
        if NORM_TOPK:
            rw = rw / rw.sum(axis=-1, keepdims=True)
        rw = rw.astype(x.dtype)
        combine = jnp.zeros((N, NUM_EXPERTS), x.dtype).at[jnp.arange(N)[:, None], sel].set(rw)
        gu = jnp.einsum('nd,edf->nef', x, w_gate_up)
        g, h = jnp.split(gu, 2, axis=-1)
        h = jax.nn.silu(g) * h
        expert_out = jnp.einsum('nef,efd,ne->nd', h, w_down, combine)
        out = expert_out + shared
        return out.reshape(B, S, D)
    x = _layernorm(x + _L0_attn_ref(x, L0_attn_qkv_w, L0_attn_qkv_b, L0_attn_proj_w, L0_attn_proj_b), axis=-1)
    x = _layernorm(x + _L0_xattn_ref(x, ctx_1024, L0_xattn_Wq, L0_xattn_bq, L0_xattn_Wk, L0_xattn_bk, L0_xattn_Wv, L0_xattn_bv), axis=-1)
    x = _layernorm(x + _L0_ffn_ref(x, L0_ffn_gate_w, L0_ffn_w_gate_up, L0_ffn_w_down, L0_ffn_shared_w_gate, L0_ffn_shared_w_up, L0_ffn_shared_w_down, L0_ffn_shared_gate_w), axis=-1)
    return x

_drawn_inputs = setup_inputs


def setup_inputs(seed=0):
    import zlib

    import numpy as np

    out = dict(_drawn_inputs(seed))
    spreads = {'L0_xattn_bq': (0.0, 0.429), 'L0_xattn_bk': (0.0, 0.8), 'L0_xattn_bv': (0.0, 0.1)}
    factors = {'L0_attn_qkv_w': 8.0,
     'L0_attn_qkv_b': 8.0,
     'L0_attn_proj_w': 6.684,
     'L0_attn_proj_b': 3.229,
     'L0_ffn_gate_w': 7.149,
     'L0_ffn_w_gate_up': 6.66,
     'L0_ffn_w_down': 6.646,
     'L0_ffn_shared_w_gate': 4.16,
     'L0_ffn_shared_w_up': 4.096,
     'L0_ffn_shared_w_down': 4.121,
     'L0_ffn_shared_gate_w': 8.0}
    for name, (base, spread) in spreads.items():
        noise = np.random.default_rng([zlib.crc32(name.encode()), seed]).standard_normal(out[name].shape)
        drawn = base * np.exp(spread * noise) if base else spread * noise
        out[name] = jnp.asarray(drawn.astype(out[name].dtype))
    for name, factor in factors.items():
        out[name] = (out[name] * factor).astype(out[name].dtype)
    return out
```

```python
from contextlib import ExitStack

import numpy as np

import concourse.bass as bass
from concourse import mybir

P = 128
ALU = mybir.AluOpType
ACT = mybir.ActivationFunctionType
AX = mybir.AxisListType
F32 = mybir.dt.float32
F32R = mybir.dt.float32r
I32 = mybir.dt.int32

NB = 16
N = 256
D = 256
H = 16
HD = D // H
TT = N // P
KC = D // P
TILES = NB * TT
GH = 4
GROUPS = H // GH
HALF = H // 2
ROWS = 96
MROW = 96
RING = 8
EPS = 1e-5
E = 16
NR = E + 2
BLOCKS = 2 * NB * N // P + E - 1
CLEAR = -(-BLOCKS // NB)
LOG_P = P.bit_length() - 1
FF = 704
FC = -(-FF // P)
FF_PAD = FC * P


class Step:

    def __init__(self, turn, c, unroll=2):
        self.turn, self.c, self.unroll, self.static = turn, c, unroll, isinstance(turn, int)
        self.n = unroll * turn + c
        self.par = c % 2

    def __add__(self, k):
        return Step(self.turn, self.c + k, self.unroll)

    def __sub__(self, k):
        return Step(self.turn, self.c - k, self.unroll)

    def least(self, k):
        return not self.static or self.n >= k

    def inside(self):
        return not self.static or 0 <= self.n < NB


class Pipeline:

    def __init__(self, first, loop0, loop1, last, users, count=NB):
        self.first, self.loop0, self.loop1, self.last, self.users, self.count = first, loop0, loop1, last, users, count
        self.bank = {name: bank for name, bank, _ in users}

    def use(self, step, name):
        mine = [u for u in self.users if u[1] == self.bank[name]]
        at = [u[0] for u in mine].index(name) + 1
        upto = step.n if step.static else self.loop0
        before = sum(0 <= i + u[2] < self.count for i in range(self.first, upto) for u in mine)
        if step.static:
            return before + sum(0 <= step.n + u[2] < self.count for u in mine[:at])
        return 2 * len(mine) * step.turn + (before + (step.c - self.loop0) * len(mine) + at)

    def steps(self, eng, body, shorter=0):
        loop1 = self.loop1 - shorter
        for i in range(self.first, self.loop0):
            body(Step(0, i))
        with eng.Fori(0, (loop1 - self.loop0) // 2) as j:
            body(Step(j, self.loop0))
            body(Step(j, self.loop0 + 1))
        for i in range(loop1, self.last + 1):
            body(Step(0, i))


def product(pe, out, lhs, rhs, chunks=KC):
    todo = [(c, l, r) for c in range(chunks) for l, r in ((0, 0), (1, 0), (0, 1))]
    for n, (c, l, r) in enumerate(todo):
        last = pe.matmul(out, lhs(l, c), rhs(r, c), start=(n == 0), stop=(n == len(todo) - 1))
    return last


def apart(eng, met):
    eng.sem_inc(met, 1)


def self_attention(nc, a, heads_dram, stacks_dram, ident, expert_rows):
    pipe = Pipeline(-1, 3, 15, NB + 1, [("MT1", 1, -1), ("QK0", 0, 1), ("QK1", 1, 1), ("V", 0, 1), ("QT", 1, 1),
                                        ("KT", 0, 1), ("MT0", 1, 0)])
    BANK, use = pipe.bank, pipe.use
    with ExitStack() as ctx:
        def sb(name, shape, dt=F32):
            return ctx.enter_context(nc.sbuf_tensor(name, [P] + shape, dt))

        def sem(name):
            return ctx.enter_context(nc.semaphore(name))

        w_qkv = sb("w_qkv", [2, KC, 3 * D], F32R)
        cos_t = sb("cos_t", [TT, 2, HD])
        sin_t = sb("sin_t", [TT, 2, HD])
        qkb = sb("qkb", [2 * D])
        roped_b = sb("roped_b", [TT, 2 * D])
        v_b = sb("v_b", [D])
        xT = [sb(f"xT{p}", [KC, N]) for p in range(2)]
        x_hl = sb("x_hl", [2, KC, N], F32R)
        t1 = sb("t1", [TT, 2 * D])
        t2 = sb("t2", [TT, 2 * D])
        q_hl = sb("q_hl", [2, KC, N], F32R)
        k_hl = sb("k_hl", [2, KC, N], F32R)
        v_st = sb("v_st", [TT, D])
        v_aug = [sb(f"v_aug{p}", [TT, H, 32]) for p in range(2)]
        q_stack = [sb(f"q_stack{p}", [H, N], F32R) for p in range(2)]
        k_stack = [sb(f"k_stack{p}", [H, N], F32R) for p in range(2)]
        neg_m = [sb(f"neg_m{c}", [TT, P]) for c in range(2)]
        m_rows = [sb(f"m_rows{c}", [N], F32R) for c in range(2)]
        probs = sb("probs", [RING, TT, N])
        o_sb = [sb(f"o_sb{p}", [GROUPS, N]) for p in range(2)]
        w_raw = sb("w_raw", [KC, 3 * D])
        no_rows = sb("no_rows", [D])

        def psum(name):
            return ctx.enter_context(nc.psum_tensor(name, [P, 512], F32))

        ps_s = [psum(f"ps_s{p}") for p in range(2)]
        ps_t = [psum(f"ps_t{p}") for p in range(2)]
        ps_o = [psum(f"ps_o{p}") for p in range(2)]
        ps_g = [psum(f"ps_g{p}") for p in range(2)]

        weights_in = sem("weights_in")
        tables_in = sem("tables_in")
        rows_zero = sem("rows_zero")
        rows_cleared = sem("rows_cleared")
        weights_hi = sem("weights_hi")
        weights_lo = sem("weights_lo")
        zeroed = sem("zeroed")
        stacks_zero = sem("stacks_zero")
        stacks_ones = sem("stacks_ones")
        q_zero = sem("q_zero")
        met_pool = sem("q_met_pool")
        bias_step = sem("bias_step")
        xT_in = [sem(f"xT_in{p}") for p in range(2)]
        x_hi = sem("x_hi")
        x_lo = sem("x_lo")
        full = [sem(f"full{g}") for g in range(2)]
        read = [sem(f"read{g}") for g in range(2)]
        rope_b = sem("rope_b")
        roped = sem("roped")
        q_hi = sem("q_hi")
        k_hi = sem("k_hi")
        v_aug_done = sem("v_aug_done")
        q_out = sem("q_out")
        k_out = sem("k_out")
        stack_in = [sem(f"stack_in{c}") for c in range(2)]
        m_in = [sem(f"m_in{c}") for c in range(2)]
        s_full = sem("s_full")
        max_done = sem("max_done")
        t_full = sem("t_full")
        exp_done = sem("exp_done")
        pv_done = sem("pv_done")
        o_read = sem("o_read")
        o_out = [sem(f"o_out{p}") for p in range(2)]

        xT_dram = a["xT"].rearrange("(c p) t -> p c t", p=P)
        heads_out = heads_dram.rearrange("(g r) t -> r g t", r=P)

        def spread(name, lo, hi):
            return a[name].rearrange("(o n) -> o n", o=1)[:, lo:hi].broadcast_to([P, hi - lo])

        block = ctx.enter_context(nc.Block())

        @block.sync
        def _(sp):
            sp.dma_start(w_raw[:], a["qkvT"].rearrange("(c p) n -> p c n", p=P)).then_inc(weights_in, 16)
            sp.dma_start(xT[0][:], xT_dram[:, :, 0:N]).then_inc(xT_in[0], 16)
            for tile, src in ((cos_t[:], a["cos"].rearrange("(t p) q d -> p t q d", p=P)),
                              (sin_t[:], a["sin"].rearrange("(t p) q d -> p t q d", p=P)),
                              (ident[:], a["ident"]),
                              (qkb[:], spread("qkv_b", 0, 2 * D)), (v_b[:], spread("qkv_b", 2 * D, 3 * D))):
                sp.dma_start(tile, src).then_inc(tables_in, 16)

            def step(i):
                p, s, t, x = i + 1, i, i - 1, i - 2
                if (p + 1).inside():
                    if p.least(1):
                        sp.wait_ge(x_lo, p.n)
                    sp.dma_start(xT[(p + 1).par][:], xT_dram[:, :, bass.ds((p + 1).n * N, N)]).then_inc(xT_in[(p + 1).par], 16)
                if t.inside():
                    sp.wait_ge(read[BANK["MT1"]], use(i, "MT1"))
                    sp.dma_start(q_stack[t.par][MROW:MROW + 1, HALF:H, :].bitcast(F32),
                                 m_rows[1][0:HALF, :].bitcast(F32)).then_inc(m_in[1], 16)
                if x.inside():
                    sp.wait_ge(o_read, GROUPS * x.n + GROUPS)
                    sp.dma_start(heads_out[:, :, bass.ds(x.n * N, N)], o_sb[x.par][:]).then_inc(o_out[x.par], 16)
                if p.inside():
                    sp.wait_ge(read[BANK["QT"]], use(i, "QT"))
                    for part in range(2):
                        sp.dma_start(stacks_dram[p.par, 0, part].rearrange("(c r) t -> r c t", r=P),
                                     q_hl[:, part].bitcast(F32)).then_inc(q_out, 16)
                    sp.wait_ge(read[BANK["KT"]], use(i, "KT"))
                    for part in range(2):
                        sp.dma_start(stacks_dram[p.par, 1, part].rearrange("(c r) t -> r c t", r=P),
                                     k_hl[:, part].bitcast(F32)).then_inc(k_out, 16)
                    if p.static and p.n < 2:
                        sp.wait_ge(stacks_ones, 2)
                        sp.wait_ge(q_zero, 2)
                    sp.wait_ge(q_out, 32 * p.n + 32)
                    sp.wait_ge(k_out, 32 * p.n + 32)

                def stack_half(c):
                    if p.least(2):
                        sp.wait_ge(t_full, t.n * H + HALF * (c + 1))
                    for kind, stack, order in ((0, q_stack, (0, 1, 0)), (1, k_stack, (0, 0, 1))):
                        for slot, part in enumerate(order):
                            rows = stacks_dram[p.par, kind, part].rearrange("(h d) t -> d h t", d=HD)
                            sp.dma_start(stack[p.par][HD * slot:HD * slot + HD, HALF * c:HALF * c + HALF, :].bitcast(F32),
                                         rows[:, HALF * c:HALF * c + HALF, :]).then_inc(stack_in[c], 16)

                if p.inside():
                    stack_half(0)
                if s.inside():
                    sp.wait_ge(read[BANK["MT0"]], use(i, "MT0"))
                    sp.dma_start(q_stack[s.par][MROW:MROW + 1, 0:HALF, :].bitcast(F32),
                                 m_rows[0][0:HALF, :].bitcast(F32)).then_inc(m_in[0], 16)
                if p.inside():
                    stack_half(1)

            pipe.steps(sp, step, 2)
            for p in range(2):
                sp.wait_ge(o_out[p], 16 * NB // 2)
            sp.wait_ge(rows_cleared, 16 * NB)

        @block.tensor
        def _(pe):
            def fill(i, name):
                before = use(i, name) - 1
                if not isinstance(before, int) or before > 0:
                    pe.wait_ge(read[BANK[name]], before)

            def turn(i, name, src):
                for o in range(2):
                    for n in range(2):
                        last = pe.transpose(ps_g[BANK[name]][:, (o * 2 + n) * P:(o * 2 + n + 1) * P], src(o, n), ident[:, :])
                last.then_inc(full[BANK[name]], 1)

            def scores_by_query(b, h):
                if h % HALF == 0:
                    pe.wait_ge(stack_in[h // HALF], 96 * b.n + 96)
                if b.least(1) or h >= 2:
                    pe.wait_ge(max_done, H * b.n + h - 1)
                for t in range(TT):
                    last = pe.matmul(ps_s[h % 2][:, t * N:(t + 1) * N], q_stack[b.par][0:ROWS, h, t * P:(t + 1) * P],
                                     k_stack[b.par][0:ROWS, h, :], start=True, stop=True)
                last.then_inc(s_full, 1)

            def scores_by_key(b, h):
                if h % HALF == 0:
                    pe.wait_ge(m_in[h // HALF], 16 * b.n + 16)
                if b.least(1) or h >= 2:
                    pe.wait_ge(exp_done, H * b.n + h - 1)
                for t in range(TT):
                    last = pe.matmul(ps_t[h % 2][:, t * N:(t + 1) * N], k_stack[b.par][0:MROW + 1, h, t * P:(t + 1) * P],
                                     q_stack[b.par][0:MROW + 1, h, :], start=True, stop=True)
                last.then_inc(t_full, 1)

            def outputs(b, g):
                pe.wait_ge(exp_done, H * b.n + GH * (g + 1))
                if g == 0:
                    pe.wait_ge(v_aug_done, b.n + 1)
                if b.least(1) or g >= 2:
                    pe.wait_ge(o_read, GROUPS * b.n + g - 1)
                for t in range(TT):
                    for j in range(GH):
                        h = GH * g + j
                        last = pe.matmul(ps_o[g % 2][32 * j:32 * j + 32, 0:N], v_aug[b.par][:, t, h, :],
                                         probs[:, h % RING, t, :], start=(t == 0), stop=(t == TT - 1))
                last.then_inc(pv_done, 1)

            def maxima_turned(i, name, c, b):
                fill(i, name)
                pe.wait_ge(max_done, H * b.n + HALF * (c + 1))
                for q in range(TT):
                    last = pe.transpose(ps_g[BANK[name]][:, q * P:(q + 1) * P], neg_m[c][:, q, :], ident[:, :])
                last.then_inc(full[BANK[name]], 1)

            def qk(i, tile, b):
                name = f"QK{tile}"
                fill(i, name)
                if tile == 0:
                    pe.wait_ge(x_hi, b.n + 1)
                    pe.wait_ge(x_lo, b.n + 1)
                product(pe, ps_g[BANK[name]][:, :], lambda l, c: x_hl[:, l, c, tile * P:(tile + 1) * P],
                        lambda r, c: w_qkv[:, r, c, 0:2 * D]).then_inc(full[BANK[name]], 1)

            pe.wait_ge(weights_lo, 1)
            pe.wait_ge(tables_in, 5 * 16)
            pe.wait_ge(zeroed, 2)

            def step(i):
                p, s, t, x = i + 1, i, i - 1, i - 2
                for n in range(H):
                    if s.inside():
                        scores_by_query(s, n)
                    if t.inside():
                        scores_by_key(t, n)
                    if n == 0 and t.inside():
                        maxima_turned(i, "MT1", 1, t)
                    if n == 1 and x.inside():
                        outputs(x, GROUPS - 1)
                    if n == 1 and p.inside():
                        qk(i, 0, p)
                    if n == 2 and p.inside():
                        qk(i, 1, p)
                    if n == 3 and p.inside():
                        fill(i, "V")
                        for q in range(TT):
                            last = product(pe, ps_g[BANK["V"]][:, q * D:(q + 1) * D],
                                           lambda l, c: x_hl[:, l, c, q * P:(q + 1) * P],
                                           lambda r, c: w_qkv[:, r, c, 2 * D:3 * D])
                        last.then_inc(full[BANK["V"]], 1)
                    if n == 5 and t.inside():
                        outputs(t, 0)
                    if n == 5 and p.inside():
                        fill(i, "QT")
                        pe.wait_ge(roped, TT * p.n + TT)
                        turn(i, "QT", lambda o, m: t1[:, m, o * P:(o + 1) * P])
                    if n == 6 and p.inside():
                        fill(i, "KT")
                        turn(i, "KT", lambda o, m: t1[:, m, D + o * P:D + (o + 1) * P])
                    if n == 8 and s.inside():
                        maxima_turned(i, "MT0", 0, s)
                    if n == 9 and t.inside():
                        outputs(t, 1)
                    if n == 13 and t.inside():
                        outputs(t, 2)

            pipe.steps(pe, step)

        @block.scalar
        def _(act):
            act.wait_ge(weights_in, 16)
            act.copy(w_qkv[:, 0], w_raw[:]).then_inc(weights_hi, 1)

            def hi_of(i, name, dst, done):
                act.wait_ge(full[BANK[name]], use(i, name))
                act.copy(dst[:, 0], ps_g[BANK[name]].rearrange("p (c t) -> p c t", c=KC)).then_inc(done, 1)

            def group_out(b, g):
                act.wait_ge(pv_done, GROUPS * b.n + g + 1)
                if g == 0 and b.least(2):
                    act.wait_ge(o_out[b.par], 16 * (b.turn + b.c // 2))
                act.copy(o_sb[b.par][:, g, :], ps_o[g % 2][:, 0:N]).then_inc(o_read, 1)

            def maxima_out(i, name, c, b):
                act.wait_ge(full[BANK[name]], use(i, name))
                if b.least(1):
                    act.wait_ge(m_in[c], 16 * b.n)
                act.copy(m_rows[c][0:HALF, :], ps_g[BANK[name]][0:HALF, 0:N]).then_inc(read[BANK[name]], 1)

            def step(i):
                p, s, t, x = i + 1, i, i - 1, i - 2
                if s.inside():
                    if s.static and s.n == 0:
                        act.wait_ge(rows_zero, 1)
                    act.dma_start(expert_rows.rearrange("(k p) d -> p k d", p=P)[:, bass.ds(s.n * CLEAR, CLEAR), :],
                                  no_rows[:].unsqueeze(1).broadcast_to([P, CLEAR, D])).then_inc(rows_cleared, 16)
                for n in range(H):
                    if n == 0 and p.inside():
                        act.wait_ge(xT_in[p.par], 16 * (p.turn + p.c // 2 + 1))
                        if p.least(1):
                            act.wait_ge(full[BANK["V"]], use(i - 1, "V"))
                        act.copy(x_hl[:, 0], xT[p.par][:]).then_inc(x_hi, 1)
                    if t.inside():
                        act.wait_ge(t_full, H * t.n + n + 1)
                        if n % GH == 0 and (t.least(1) or n >= RING):
                            act.wait_ge(pv_done, GROUPS * t.n + n // GH - 1)
                        act.activation(probs[:, n % RING], ps_t[n % 2].rearrange("p (t q) -> p t q", t=TT),
                                       ACT.Exp).then_inc(exp_done, 1)
                    if n == 0 and t.inside():
                        maxima_out(i, "MT1", 1, t)
                    if n == 1 and x.inside():
                        group_out(x, GROUPS - 1)
                    if n == 5 and t.inside():
                        group_out(t, 0)
                    if n == 5 and p.inside():
                        if p.least(1):
                            act.wait_ge(q_out, 32 * p.n)
                        hi_of(i, "QT", q_hl, q_hi)
                    if n == 6 and p.inside():
                        if p.least(1):
                            act.wait_ge(k_out, 32 * p.n)
                        hi_of(i, "KT", k_hl, k_hi)
                    if n == 8 and s.inside():
                        maxima_out(i, "MT0", 0, s)
                    if n == 9 and t.inside():
                        group_out(t, 1)
                    if n == 13 and t.inside():
                        group_out(t, 2)

            pipe.steps(act, step)

        @block.vector
        def _(dve):
            for c in range(2):
                dve.memset(neg_m[c][:], 0.0)
            for p in range(2):
                last = dve.memset(v_aug[p][:, :, :, HD:32], 0.0)
            last.then_inc(zeroed, 1)
            dve.wait_ge(zeroed, 1)
            for p in range(2):
                last = dve.memset(v_aug[p][:, :, :, HD:HD + 1], 1.0)
            last.then_inc(zeroed, 1)
            dve.wait_ge(zeroed, 2)
            dve.wait_ge(weights_hi, 1)
            dve.tensor_tensor(w_qkv[:, 1], w_raw[:], w_qkv[:, 0].bitcast(F32), ALU.subtract).then_inc(weights_lo, 1)

            def rotate(out, src, tile):
                o = out.rearrange("p (q h d) -> p q h d", q=2, d=HD)
                s = src.rearrange("p (q h d) -> p q h d", q=2, d=HD)
                w = sin_t[:, tile].unsqueeze(2).broadcast_to([P, 2, H, HD])
                dve.tensor_tensor(o[:, :, :, 0:HD // 2], s[:, :, :, HD // 2:HD], w[:, :, :, 0:HD // 2], ALU.mult)
                return dve.tensor_tensor(o[:, :, :, HD // 2:HD], s[:, :, :, 0:HD // 2], w[:, :, :, HD // 2:HD], ALU.mult)

            def times_cos(out, src, tile):
                return dve.tensor_tensor(out.rearrange("p (q h d) -> p q h d", q=2, d=HD),
                                         src.rearrange("p (q h d) -> p q h d", q=2, d=HD),
                                         cos_t[:, tile].unsqueeze(2).broadcast_to([P, 2, H, HD]), ALU.mult)

            for p in range(2):
                dve.memset(q_stack[p][:].bitcast(F32), 0.0).then_inc(q_zero, 1)

            dve.wait_ge(tables_in, 5 * 16)
            for tile in range(TT):
                times_cos(roped_b[:, tile], qkb[:], tile)
                rotate(t2[:, 0], qkb[:], tile).then_inc(bias_step, 1)
                dve.wait_ge(bias_step, 2 * tile + 1)
                dve.tensor_tensor(roped_b[:, tile], roped_b[:, tile], t2[:, 0], ALU.add).then_inc(bias_step, 1)
                dve.wait_ge(bias_step, 2 * tile + 2)

            def fetch(i, name):
                dve.wait_ge(full[BANK[name]], use(i, name))
                return ps_g[BANK[name]]

            def lo_of(i, name, hl, hi_done, b):
                dve.wait_ge(hi_done, b.n + 1)
                bank = fetch(i, name)
                dve.tensor_tensor(hl[:, 1], bank.rearrange("p (c t) -> p c t", c=KC), hl[:, 0].bitcast(F32),
                                  ALU.subtract).then_inc(read[BANK[name]], 1)

            def rope(i, tile, b):
                bank = fetch(i, f"QK{tile}")
                if b.least(1):
                    dve.wait_ge(roped, TT * b.n)
                times_cos(t1[:, tile], bank[:], tile)
                rotate(t2[:, tile], bank[:], tile).then_inc(read[BANK[f"QK{tile}"]], 1)

            def step(i):
                p, s, t, x = i + 1, i, i - 1, i - 2
                for n in range(H):
                    if s.inside():
                        dve.wait_ge(s_full, H * s.n + n + 1)
                        c = n // HALF
                        if n % HALF == 0 and s.least(1):
                            if c == 0:
                                dve.wait_ge(full[BANK["MT0"]], use(i - 1, "MT0"))
                            else:
                                dve.wait_ge(full[BANK["MT1"]], use(i, "MT1"))
                        dve.tensor_reduce(neg_m[c][:, :, n % HALF], ps_s[n % 2].rearrange("p (t k) -> p t k", t=TT),
                                          AX.X, ALU.max, negate=True).then_inc(max_done, 1)
                    if n == 1 and p.inside():
                        rope(i, 0, p)
                    if n == 2 and p.inside():
                        rope(i, 1, p)
                    if n == 3 and p.inside():
                        bank = fetch(i, "V")
                        if p.least(1):
                            dve.wait_ge(v_aug_done, p.n)
                        dve.tensor_tensor(v_st[:], bank.rearrange("p (t d) -> p t d", t=TT),
                                          v_b[:].unsqueeze(1).broadcast_to([P, TT, D]), ALU.add).then_inc(read[BANK["V"]], 1)
                    if n == 5 and p.inside():
                        lo_of(i, "QT", q_hl, q_hi, p)
                    if n == 6 and p.inside():
                        lo_of(i, "KT", k_hl, k_hi, p)

            pipe.steps(dve, step)

        @block.gpsimd
        def _(pool):
            pool.memset(no_rows[:], 0.0).then_inc(rows_zero, 1)
            for p in range(2):
                pool.memset(k_stack[p][:].bitcast(F32), 0.0).then_inc(stacks_zero, 1)
            pool.wait_ge(stacks_zero, 2)
            for p in range(2):
                pool.memset(k_stack[p][MROW:MROW + 1, :, :].bitcast(F32), 1.0).then_inc(stacks_ones, 1)
            pool.wait_ge(stacks_ones, 2)

            def step(i):
                p, s, t, x = i + 1, i, i - 1, i - 2
                if p.inside():
                    pool.wait_ge(x_hi, p.n + 1)
                    pool.tensor_tensor(x_hl[:, 1], xT[p.par][:], x_hl[:, 0].bitcast(F32), ALU.subtract).then_inc(x_lo, 1)
                if s.inside():
                    if s.least(2):
                        pool.wait_ge(pv_done, GROUPS * s.n - GROUPS)
                    pool.wait_ge(read[BANK["V"]], use(i - 1, "V"))
                    if s.static and s.n < 2:
                        pool.wait_ge(zeroed, 2)
                    apart(pool, met_pool)
                    pool.tensor_copy(v_aug[s.par][:, :, :, 0:HD],
                                     v_st.rearrange("p t (h d) -> p t h d", d=HD)).then_inc(v_aug_done, 1)
                if p.inside():
                    for tile in range(TT):
                        pool.wait_ge(read[BANK[f"QK{tile}"]], use(i, f"QK{tile}"))
                        pool.tensor_tensor(t1[:, tile], t1[:, tile], t2[:, tile], ALU.add).then_inc(rope_b, 1)
                        pool.wait_ge(rope_b, TT * p.n + tile + 1)
                        if p.static and p.n == 0:
                            pool.wait_ge(bias_step, 2 * tile + 2)
                        pool.tensor_tensor(t1[:, tile], t1[:, tile], roped_b[:, tile], ALU.add).then_inc(roped, 1)

            pipe.steps(pool, step)


def cross_attention(nc, a, heads_dram, x2_all, x2T_hl, logits, ident):
    pipe = Pipeline(0, 2, 16, NB + 1, [("AT", 0, 0), ("LG", 6, -2), ("S2", 1, -1), ("PJ", 2, 0), ("P2T", 3, -1),
                                       ("XK", 4, 0), ("PV2", 5, -1), ("X1T", 0, 0), ("XV", 7, 0), ("XQ", 2, 0),
                                       ("X2T", 3, -1)])
    bank, use = pipe.bank, pipe.use
    with ExitStack() as ctx:
        def sb(name, shape, dt=F32):
            return ctx.enter_context(nc.sbuf_tensor(name, [P] + shape, dt))

        def sem(name):
            return ctx.enter_context(nc.semaphore(name))

        w_pj = sb("w_pj", [2, KC, D], F32R)
        w_xq = sb("w_xq", [2, KC, D], F32R)
        w_xk = sb("w_xk", [2, KC, D], F32R)
        w_xv = sb("w_xv", [2, KC, D], F32R)
        w_rt = sb("w_rt", [2, KC, P], F32R)
        w_raw = sb("x_w_raw", [4 * KC * D + KC * P])
        pj_b = sb("pj_b", [D])
        xv_b = sb("xv_b", [D])
        xq_b = sb("xq_b", [KC])
        xk_b = sb("xk_b", [KC])
        minus_half = sb("minus_half", [TT])
        heads = [sb(f"heads{p}", [TT, HD + 1, HD]) for p in range(2)]
        cT = [sb(f"cT{p}", [KC, N]) for p in range(2)]
        xr = [sb(f"xr{p}", [TT, D]) for p in range(2)]
        c_hl = sb("c_hl", [2, KC, N], F32R)
        xb = sb("xb", [TT, D])
        rec = sb("rec", [TT, HD])
        att = sb("att", [TT, D])
        att_hl = sb("att_hl", [2, KC, N], F32R)
        x1 = [sb(f"x1_{p}", [TT, D]) for p in range(2)]
        x1_hl = sb("x1_hl", [2, KC, N], F32R)
        stats = sb("stats", [2, TT, 6])
        mv = sb("mv", [2, TT, 2])
        var_e = sb("var_e", [2, TT])
        rstd = sb("rstd", [2, TT])
        xk_f = sb("xk_f", [KC, N])
        xk_hl = sb("xk_hl", [2, KC, N], F32R)
        xq_f = sb("xq_f", [KC, N])
        xq_hl = sb("xq_hl", [2, KC, N], F32R)
        xv = sb("xv", [TT, D])
        neg_m2 = sb("neg_m2", [TT])
        sum2 = sb("sum2", [TT])
        rec2 = sb("rec2", [TT])
        p2 = sb("p2", [TT, N])
        p2T = sb("p2T", [TT, N])
        x2 = sb("x2", [TT, D])
        x2_hl = sb("x2_hl", [2, KC, N], F32R)
        ps = [ctx.enter_context(nc.psum_tensor(f"ps_x{g}", [P, 512], F32)) for g in range(8)]

        weights_in = sem("x_weights_in")
        tables_in = sem("x_tables_in")
        weights_hi = sem("x_weights_hi")
        weights_lo = sem("x_weights_lo")
        consts = sem("consts")
        met_dve = sem("c_met_dve")
        met_pool = sem("c_met_pool")
        heads_in = [sem(f"heads_in{p}") for p in range(2)]
        cT_in = [sem(f"cT_in{p}") for p in range(2)]
        xr_in = [sem(f"xr_in{p}") for p in range(2)]
        full = [sem(f"x_full{g}") for g in range(8)]
        read = [sem(f"x_read{g}") for g in range(8)]
        c_hi = sem("c_hi")
        c_lo = sem("c_lo")
        xb_done = sem("xb_done")
        rec_done = sem("rec_done")
        att_done = sem("att_done")
        att_hi = sem("att_hi")
        stats_done = [sem(f"stats_done{w}") for w in range(2)]
        mv_done = [sem(f"mv_done{w}") for w in range(2)]
        var_done = [sem(f"var_done{w}") for w in range(2)]
        rstd_done = [sem(f"rstd_done{w}") for w in range(2)]
        x1_done = sem("x1_done")
        x1_hi = sem("x1_hi")
        xk_hi = sem("xk_hi")
        xk_lo = sem("xk_lo")
        xq_hi = sem("xq_hi")
        xq_lo = sem("xq_lo")
        max2_done = sem("max2_done")
        rec2_done = sem("rec2_done")
        x2_done = sem("x2_done")
        x2_hi = sem("x2_hi")
        x2_out = sem("x2_out")
        x2T_out = sem("x2T_out")

        staged, at = [], 0
        for name, dst in (("projT", w_pj), ("WkT", w_xk), ("WvT", w_xv), ("WqT", w_xq), ("routerT", w_rt)):
            cols = dst.shape[3]
            staged.append((name, dst, w_raw[:, at:at + KC * cols].rearrange("p (c n) -> p c n", c=KC)))
            at += KC * cols

        heads_in_dram = heads_dram.rearrange("(h d) (r w) -> h r d w", h=H, w=HD)
        cT_dram = a["ctxT"].rearrange("(c p) t -> p c t", p=P)
        x_dram = a["x"].rearrange("b (t p) d -> b p t d", p=P)

        def spread(name):
            return a[name].rearrange("(o n) -> o n", o=1).broadcast_to([P, D])

        def one(ap, b, how):
            return ap[bass.ds(b.n, 1)].rearrange(how)

        block = ctx.enter_context(nc.Block())

        @block.sync
        def _(sp):
            for name, dst, raw in staged:
                sp.dma_start(raw, a[name].rearrange("(c p) n -> p c n", p=P)).then_inc(weights_in, 16)
            for tile, src in ((pj_b[:], spread("proj_b")), (xv_b[:], spread("bv")), (xq_b[:], a["bq2"]), (xk_b[:], a["bk2"])):
                sp.dma_start(tile, src).then_inc(tables_in, 16)

            def load(b):
                if b.least(2):
                    sp.wait_ge(att_done, b.n - 1)
                    sp.wait_ge(c_lo, b.n - 1)
                    sp.wait_ge(xb_done, b.n - 1)
                for t in range(TT):
                    sp.dma_start(heads[b.par][:, t], one(heads_in_dram, b, "o r d w -> r (o d) w")[t * P:(t + 1) * P, 0:HD + 1]
                                 ).then_inc(heads_in[b.par], 16)
                sp.dma_start(cT[b.par][:], cT_dram[:, :, bass.ds(b.n * N, N)]).then_inc(cT_in[b.par], 16)
                sp.dma_start(xr[b.par][:], one(x_dram, b, "o p t d -> p (o t) d")).then_inc(xr_in[b.par], 16)

            def step(i):
                b = i - 1
                if i.static and i.n == 0:
                    load(i)
                if (i + 1).inside():
                    load(i + 1)
                if b.inside():
                    sp.wait_ge(x2_done, TT * b.n + TT)
                    sp.dma_start(x2_all[:, bass.ds(b.n * TT, TT), :], x2[:]).then_inc(x2_out, 16)
                    sp.wait_ge(read[bank["X2T"]], use(i, "X2T"))
                    for part in range(2):
                        sp.dma_start(x2T_hl[part].rearrange("(c p) t -> p c t", p=P)[:, :, bass.ds(b.n * N, N)],
                                     x2_hl[:, part].bitcast(F32)).then_inc(x2T_out, 16)

            pipe.steps(sp, step, 2)
            sp.wait_ge(x2_out, 16 * NB)
            sp.wait_ge(x2T_out, 32 * NB)

        @block.tensor
        def _(pe):
            def fill(i, name):
                before = use(i, name) - 1
                if not isinstance(before, int) or before > 0:
                    pe.wait_ge(read[bank[name]], before)
                return ps[bank[name]]

            def turn(i, name, out, src):
                for o in range(2):
                    for n in range(2):
                        last = pe.transpose(out[:, (o * 2 + n) * P:(o * 2 + n + 1) * P], src(o, n), ident[:, :])
                last.then_inc(full[bank[name]], 1)

            def halves(i, name, out, width, lhs, rhs):
                for q in range(2):
                    last = product(pe, out[:, q * width:(q + 1) * width], lambda l, c: lhs(l, c, q), lambda r, c: rhs(r, c))
                last.then_inc(full[bank[name]], 1)

            def part(m, q):
                return slice(q * P, (q + 1) * P)

            pe.wait_ge(weights_lo, len(staged))

            def step(i):
                s, b, r = i, i - 1, i - 2
                if s.inside():
                    out = fill(i, "AT")
                    pe.wait_ge(att_done, s.n + 1)
                    turn(i, "AT", out, lambda o, m: att[:, m, o * P:(o + 1) * P])
                if b.inside():
                    out = fill(i, "S2")
                    pe.wait_ge(xk_lo, b.n + 1)
                    pe.wait_ge(xq_lo, b.n + 1)
                    halves(i, "S2", out, N, lambda l, c, q: xq_hl[:, l, c, q * P:(q + 1) * P], lambda r, c: xk_hl[:, r, c, :])
                if s.inside():
                    out = fill(i, "PJ")
                    pe.wait_ge(read[bank["AT"]], use(i, "AT"))
                    halves(i, "PJ", out, D, lambda l, c, q: att_hl[:, l, c, q * P:(q + 1) * P], lambda r, c: w_pj[:, r, c, :])
                if b.inside():
                    out = fill(i, "P2T")
                    pe.wait_ge(read[bank["S2"]], use(i, "S2"))
                    turn(i, "P2T", out, lambda o, m: p2[:, m, o * P:(o + 1) * P])
                if s.inside():
                    out = fill(i, "XK")
                    pe.wait_ge(c_hi, s.n + 1)
                    pe.wait_ge(c_lo, s.n + 1)
                    halves(i, "XK", out, N, lambda l, c, q: w_xk[:, l, c, q * P:(q + 1) * P], lambda r, c: c_hl[:, r, c, :])
                if b.inside():
                    out = fill(i, "PV2")
                    pe.wait_ge(read[bank["XV"]], use(i - 1, "XV"))
                    pe.wait_ge(read[bank["P2T"]], use(i, "P2T"))
                    for q in range(TT):
                        for k in range(TT):
                            last = pe.matmul(out[:, q * D:(q + 1) * D], p2T[:, k, q * P:(q + 1) * P], xv[:, k, :],
                                             start=(k == 0), stop=(k == TT - 1))
                    last.then_inc(full[bank["PV2"]], 1)
                if s.inside():
                    out = fill(i, "X1T")
                    pe.wait_ge(x1_done, TT * s.n + TT)
                    turn(i, "X1T", out, lambda o, m: x1[s.par][:, m, o * P:(o + 1) * P])
                    out = fill(i, "XV")
                    halves(i, "XV", out, D, lambda l, c, q: c_hl[:, l, c, q * P:(q + 1) * P], lambda r, c: w_xv[:, r, c, :])
                if r.inside():
                    out = fill(i, "LG")
                    pe.wait_ge(read[bank["X2T"]], use(i - 1, "X2T"))
                    halves(i, "LG", out, P, lambda l, c, q: x2_hl[:, l, c, q * P:(q + 1) * P], lambda r, c: w_rt[:, r, c, :])
                if s.inside():
                    out = fill(i, "XQ")
                    pe.wait_ge(read[bank["X1T"]], use(i, "X1T"))
                    halves(i, "XQ", out, N, lambda l, c, q: w_xq[:, l, c, q * P:(q + 1) * P], lambda r, c: x1_hl[:, r, c, :])
                if b.inside():
                    out = fill(i, "X2T")
                    pe.wait_ge(x2_done, TT * b.n + TT)
                    turn(i, "X2T", out, lambda o, m: x2[:, m, o * P:(o + 1) * P])

            pipe.steps(pe, step)

        @block.scalar
        def _(act):
            act.wait_ge(weights_in, 16 * len(staged))
            for _, dst, raw in staged:
                act.copy(dst[:, 0], raw).then_inc(weights_hi, 1)
            act.wait_ge(consts, 2)

            def fetch(i, name):
                act.wait_ge(full[bank[name]], use(i, name))
                return ps[bank[name]]

            def hi_of(i, name, dst, done):
                act.copy(dst[:, 0], fetch(i, name).rearrange("p (c t) -> p c t", c=KC)).then_inc(done, 1)

            def context_hi(b):
                act.wait_ge(cT_in[b.par], 16 * (b.turn + b.c // 2 + 1))
                act.copy(c_hl[:, 0], cT[b.par][:]).then_inc(c_hi, 1)

            def step(i):
                s, b = i, i - 1
                if s.inside():
                    if s.least(1):
                        act.wait_ge(full[bank["XV"]], use(i - 1, "XV"))
                    context_hi(s)
                    if s.least(1):
                        act.wait_ge(full[bank["PJ"]], use(i - 1, "PJ"))
                    hi_of(i, "AT", att_hl, att_hi)
                if b.inside():
                    act.wait_ge(max2_done, b.n + 1)
                    if b.least(1):
                        act.wait_ge(full[bank["P2T"]], use(i - 1, "P2T"))
                        act.wait_ge(rec2_done, b.n)
                    out = fetch(i, "S2")
                    for q in range(TT):
                        last = act.activation(p2[:, q, :], out[:, q * N:(q + 1) * N], ACT.Exp, bias=neg_m2[:, q:q + 1],
                                              accum_out=sum2[:, q:q + 1])
                    last.then_inc(read[bank["S2"]], 1)
                    if b.least(1):
                        act.wait_ge(full[bank["PV2"]], use(i - 1, "PV2"))
                    act.copy(p2T[:], fetch(i, "P2T").rearrange("p (k q) -> p k q", k=TT)).then_inc(read[bank["P2T"]], 1)
                if s.inside():
                    if s.least(1):
                        act.wait_ge(xk_lo, s.n)
                        act.wait_ge(xk_hi, s.n)
                    out = fetch(i, "XK")
                    for e in range(KC):
                        last = act.activation(xk_f[:, e, :], out[:, e * N:(e + 1) * N], ACT.Identity, bias=xk_b[:, e:e + 1])
                    last.then_inc(read[bank["XK"]], 1)
                    if s.least(1):
                        act.wait_ge(full[bank["XQ"]], use(i - 1, "XQ"))
                    hi_of(i, "X1T", x1_hl, x1_hi)
                    if s.least(1):
                        act.wait_ge(xq_lo, s.n)
                    out = fetch(i, "XQ")
                    for e in range(KC):
                        last = act.activation(xq_f[:, e, :], out[:, e * N:(e + 1) * N], ACT.Identity,
                                              bias=xq_b[:, e:e + 1], scale=float(D) ** -0.5)
                    last.then_inc(read[bank["XQ"]], 1)
                if b.inside():
                    if b.least(1):
                        act.wait_ge(x2T_out, 32 * b.n)
                        act.wait_ge(full[bank["LG"]], use(i, "LG"))
                    hi_of(i, "X2T", x2_hl, x2_hi)

            pipe.steps(act, step)

        @block.vector
        def _(dve):
            dve.memset(minus_half[:], -0.5).then_inc(consts, 1)
            dve.wait_ge(tables_in, 4 * 16)
            dve.tensor_scalar(xq_b[:], xq_b[:], float(D) ** -0.5, None, ALU.mult).then_inc(consts, 1)
            for n, (_, dst, raw) in enumerate(staged):
                dve.wait_ge(weights_hi, n + 1)
                dve.tensor_tensor(dst[:, 1], raw, dst[:, 0].bitcast(F32), ALU.subtract).then_inc(weights_lo, 1)

            def fetch(i, name):
                dve.wait_ge(full[bank[name]], use(i, name))
                return ps[bank[name]]

            def lo_of(i, name, hl, hi_done, b):
                dve.wait_ge(hi_done, b.n + 1)
                out = fetch(i, name)
                dve.tensor_tensor(hl[:, 1], out.rearrange("p (c t) -> p c t", c=KC), hl[:, 0].bitcast(F32),
                                  ALU.subtract).then_inc(read[bank[name]], 1)

            def norm_stats(which, v, b):
                for q in range(TT):
                    last = dve.bn_stats(stats[:, which, q, :], v[:, q, :])
                last.then_inc(stats_done[which], 1)
                dve.wait_ge(stats_done[which], b.n + 1)
                apart(dve, met_dve)
                for q in range(TT):
                    last = dve.bn_aggr(mv[:, which, q, :], stats[:, which, q, :])
                last.then_inc(mv_done[which], 1)

            def norm_apply(which, v, b, done):
                dve.wait_ge(rstd_done[which], b.n + 1)
                dve.wait_ge(mv_done[which], b.n + 1)
                for q in range(TT):
                    dve.tensor_scalar(v[:, q, :], v[:, q, :], mv[:, which, q, 0:1], rstd[:, which, q:q + 1],
                                      ALU.subtract, ALU.mult).then_inc(done, 1)

            def heads_normed(b):
                dve.wait_ge(heads_in[b.par], 16 * TT * (b.turn + b.c // 2 + 1))
                dve.reciprocal(rec[:], heads[b.par][:, :, HD, :]).then_inc(rec_done, 1)
                dve.wait_ge(rec_done, b.n + 1)
                if b.least(1):
                    dve.wait_ge(full[bank["AT"]], use(b - 1, "AT"))
                for t in range(TT):
                    last = dve.tensor_tensor(att[:, t].rearrange("p (d w) -> p d w", w=HD), heads[b.par][:, t, 0:HD, :],
                                             rec[:, t].unsqueeze(1).broadcast_to([P, HD, HD]), ALU.mult)
                last.then_inc(att_done, 1)

            def step(i):
                s, b, r = i, i - 1, i - 2
                if i.static and i.n == 0:
                    heads_normed(i)
                if s.inside():
                    lo_of(i, "AT", att_hl, att_hi, s)
                if b.inside():
                    if b.least(1):
                        dve.wait_ge(read[bank["S2"]], use(i - 1, "S2"))
                    dve.tensor_reduce(neg_m2[:], fetch(i, "S2").rearrange("p (t k) -> p t k", t=TT), AX.X, ALU.max,
                                      negate=True).then_inc(max2_done, 1)
                if s.inside():
                    dve.wait_ge(xb_done, s.n + 1)
                    dve.tensor_tensor(x1[s.par][:], fetch(i, "PJ").rearrange("p (t d) -> p t d", t=TT), xb[:],
                                      ALU.add).then_inc(read[bank["PJ"]], 1)
                    dve.wait_ge(read[bank["PJ"]], use(i, "PJ"))
                    norm_stats(0, x1[s.par], s)
                if b.inside():
                    dve.wait_ge(read[bank["S2"]], use(i, "S2"))
                    dve.reciprocal(rec2[:], sum2[:]).then_inc(rec2_done, 1)
                if s.inside():
                    norm_apply(0, x1[s.par], s, x1_done)
                    dve.wait_ge(read[bank["XK"]], use(i, "XK"))
                    dve.tensor_copy(xk_hl[:, 0], xk_f[:]).then_inc(xk_hi, 1)
                if b.inside():
                    dve.wait_ge(rec2_done, b.n + 1)
                    out = fetch(i, "PV2")
                    if b.least(1):
                        dve.wait_ge(x2_out, 16 * b.n)
                    for q in range(TT):
                        last = dve.scalar_tensor_tensor(out=x2[:, q, :], in0=out[:, q * D:(q + 1) * D],
                                                        scalar=rec2[:, q:q + 1], in1=x1[b.par][:, q, :],
                                                        op0=ALU.mult, op1=ALU.add)
                    last.then_inc(read[bank["PV2"]], 1)
                    dve.wait_ge(read[bank["PV2"]], use(i, "PV2"))
                    norm_stats(1, x2, b)
                if s.inside():
                    lo_of(i, "X1T", x1_hl, x1_hi, s)
                    dve.tensor_tensor(xv[:], fetch(i, "XV").rearrange("p (t d) -> p t d", t=TT),
                                      xv_b[:].unsqueeze(1).broadcast_to([P, TT, D]), ALU.add).then_inc(read[bank["XV"]], 1)
                if r.inside():
                    dve.tensor_copy(logits[:, bass.ds(r.n * TT, TT), :],
                                    fetch(i, "LG")[:, 0:TT * P].rearrange("p (t e) -> p t e", t=TT)[:, :, 0:NR]).then_inc(read[bank["LG"]], 1)
                if b.inside():
                    norm_apply(1, x2, b, x2_done)
                if (i + 1).inside() and s.inside():
                    heads_normed(i + 1)
                if s.inside():
                    dve.wait_ge(read[bank["XQ"]], use(i, "XQ"))
                    dve.tensor_copy(xq_hl[:, 0], xq_f[:]).then_inc(xq_hi, 1)
                    dve.wait_ge(xq_hi, s.n + 1)
                    dve.tensor_tensor(xq_hl[:, 1], xq_f[:], xq_hl[:, 0].bitcast(F32), ALU.subtract).then_inc(xq_lo, 1)
                if b.inside():
                    lo_of(i, "X2T", x2_hl, x2_hi, b)

            pipe.steps(dve, step, 2)

        @block.gpsimd
        def _(pool):
            def norm_root(which, b):
                pool.wait_ge(mv_done[which], b.n + 1)
                if b.least(1):
                    pool.wait_ge(x2_done if which else x1_done, TT * b.n)
                apart(pool, met_pool)
                pool.tensor_scalar(var_e[:, which], mv[:, which, :, 1], EPS, None, ALU.add).then_inc(var_done[which], 1)
                pool.wait_ge(var_done[which], b.n + 1)
                pool.tensor_tensor(rstd[:, which], var_e[:, which], minus_half[:], ALU.pow).then_inc(rstd_done[which], 1)

            def step(i):
                s, b = i, i - 1
                if s.inside():
                    pool.wait_ge(c_hi, s.n + 1)
                    pool.tensor_tensor(c_hl[:, 1], cT[s.par][:], c_hl[:, 0].bitcast(F32), ALU.subtract).then_inc(c_lo, 1)
                    pool.wait_ge(xr_in[s.par], 16 * (s.turn + s.c // 2 + 1))
                    if s.least(1):
                        pool.wait_ge(read[bank["PJ"]], use(i - 1, "PJ"))
                    pool.tensor_tensor(xb[:], xr[s.par][:], pj_b[:].unsqueeze(1).broadcast_to([P, TT, D]), ALU.add).then_inc(xb_done, 1)
                    norm_root(0, s)
                if b.inside():
                    norm_root(1, b)
                if s.inside():
                    pool.wait_ge(xk_hi, s.n + 1)
                    pool.tensor_tensor(xk_hl[:, 1], xk_f[:], xk_hl[:, 0].bitcast(F32), ALU.subtract).then_inc(xk_lo, 1)

            pool.wait_ge(tables_in, 4 * 16)
            pool.wait_ge(consts, 1)
            pipe.steps(pool, step)


def routing(nc, a, logits, w_gu, w_dn, w_sgu, w_sdn, pos, block_expert, w_top, w_shared):
    RAWS = 2
    BY_POOL = 10
    with ExitStack() as ctx:
        def sb(name, shape, dt=F32):
            return ctx.enter_context(nc.sbuf_tensor(name, [P] + shape, dt))

        def sem(name):
            return ctx.enter_context(nc.semaphore(name))

        tri = sb("tri", [P])
        ones = sb("ones", [P])
        falling = sb("falling", [E])
        blocks = sb("blocks", [BLOCKS])
        top1 = sb("top1", [TILES])
        top2 = sb("top2", [TILES])
        first = sb("first", [TILES])
        hit = sb("hit", [TILES, E])
        rest = sb("rest", [TILES, E])
        one1 = sb("one1", [TILES, E])
        one2 = sb("one2", [TILES, E])
        both = sb("both", [TILES, E])
        upto = [sb(f"upto{p}", [TILES, E]) for p in range(2)]
        rows = sb("rows", [TILES, E])
        count_i = sb("count_i", [E], I32)
        room = sb("room", [E])
        end = [sb(f"end{p}", [E]) for p in range(2)]
        before = sb("before", [BLOCKS, E])
        ended = sb("ended", [BLOCKS])
        gap = sb("gap", [TILES])
        gap_exp = sb("gap_exp", [TILES])
        gate_exp = sb("gate_exp", [TILES])
        raw = [sb(f"raw{p}", [FC * D]) for p in range(RAWS)]
        ps_before = ctx.enter_context(nc.psum_tensor("ps_before", [P, TILES, E], F32))
        ps_total = ctx.enter_context(nc.psum_tensor("ps_total", [P, TILES, E], F32))

        consts_in = sem("consts_in")
        raw_in = [sem(f"raw_in{p}") for p in range(RAWS)]
        raw_hi = sem("raw_hi")
        raw_lo = sem("raw_lo")
        raw_lo_dve = sem("raw_lo_dve")
        routed = sem("routed")
        ones_set = sem("ones_set")
        gap_ready = sem("gap_ready")
        exps_done = sem("exps_done")
        both_ready = sem("both_ready")
        counted = sem("counted")

        pieces = []

        def piece(src, dst, cols, how, **sizes):
            pieces.append((src, dst, cols, how, sizes))

        for c in range(KC):
            piece(a["shared_guT"].rearrange("(c p) n -> c p n", p=P)[c], lambda r, c=c: w_sgu[:, r, c, :], 2 * FF_PAD, "p n -> p n")
        piece(a["shared_dnT"].rearrange("(c p) n -> p c n", p=P), lambda r: w_sdn[:, r], FC * D, "p (c n) -> p c n", c=FC)
        for e in range(0, E, 4):
            for c in range(KC):
                piece(a["w_gate_up"].rearrange("e (c p) n -> c p e n", p=P)[c][:, e:e + 4], lambda r, e=e, c=c: w_gu[:, e:e + 4, r, c, :],
                      4 * D, "p (e n) -> p e n", e=4)
        for e in range(0, E, 4):
            piece(a["w_down"][e:e + 4].rearrange("e p n -> p e n"), lambda r, e=e: w_dn[:, e:e + 4, r], 4 * D, "p (e n) -> p e n", e=4)

        def view(n):
            _, _, cols, how, sizes = pieces[n]
            v = raw[n % RAWS][:, 0:cols]
            return v.rearrange(how, **sizes) if sizes else v

        block = ctx.enter_context(nc.Block())

        @block.sync
        def _(sp):
            for tile, src in ((tri, a["tri"]), (falling, a["falling"]), (blocks, a["blocks"])):
                sp.dma_start(tile[:], src).then_inc(consts_in, 16)
            for n in range(len(pieces)):
                if n >= RAWS:
                    sp.wait_ge(raw_lo, min(n - RAWS + 1, BY_POOL))
                if n - RAWS >= BY_POOL:
                    sp.wait_ge(raw_lo_dve, n - RAWS + 1 - BY_POOL)
                sp.dma_start(view(n), pieces[n][0]).then_inc(raw_in[n % RAWS], 16)

        @block.scalar
        def _(act):
            act.activation(gate_exp[:], logits[:, :, E], ACT.Exp, scale=-1.0).then_inc(exps_done, 1)
            for n in range(len(pieces)):
                act.wait_ge(raw_in[n % RAWS], 16 * (n // RAWS + 1))
                act.copy(pieces[n][1](0), view(n)).then_inc(raw_hi, 1)
                if n == 3:
                    act.wait_ge(gap_ready, 1)
                    act.activation(gap_exp[:], gap[:], ACT.Exp).then_inc(exps_done, 1)

        @block.gpsimd
        def _(pool):
            pool.memset(ones[:], 1.0).then_inc(ones_set, 1)
            for n in range(BY_POOL):
                pool.wait_ge(raw_hi, n + 1)
                pool.tensor_tensor(pieces[n][1](1), view(n), pieces[n][1](0).bitcast(F32), ALU.subtract).then_inc(raw_lo, 1)

        @block.tensor
        def _(pe):
            pe.wait_ge(both_ready, 1)
            pe.wait_ge(ones_set, 1)
            pe.wait_ge(consts_in, 3 * 16)
            pe.matmul(ps_before[:, :, :], tri[:], both[:, :, :], start=True, stop=True).then_inc(counted, 1)
            pe.matmul(ps_total[:, :, :], ones[:], both[:, :, :], start=True, stop=True).then_inc(counted, 1)

        @block.vector
        def _(dve):
            def each(v):
                return v[:].unsqueeze(2).broadcast_to([P, TILES, E])

            expert_logits = logits[:, :, 0:E]
            fall = falling[:].unsqueeze(1).broadcast_to([P, TILES, E])
            dve.wait_ge(consts_in, 3 * 16)
            dve.tensor_reduce(top1[:], expert_logits, AX.X, ALU.max).then_inc(routed, 1)
            dve.wait_ge(routed, 1)
            dve.tensor_tensor(hit[:], expert_logits, each(top1), ALU.is_equal).then_inc(routed, 1)
            dve.wait_ge(routed, 2)
            dve.tensor_tensor(hit[:], hit[:], fall, ALU.mult).then_inc(routed, 1)
            dve.wait_ge(routed, 3)
            dve.tensor_reduce(first[:], hit[:], AX.X, ALU.max).then_inc(routed, 1)
            dve.wait_ge(routed, 4)
            dve.tensor_tensor(one1[:], fall, each(first), ALU.is_equal).then_inc(routed, 1)
            dve.wait_ge(routed, 5)
            dve.scalar_tensor_tensor(out=rest[:], in0=one1[:], scalar=-3.0e38, in1=expert_logits, op0=ALU.mult,
                                     op1=ALU.add).then_inc(routed, 1)
            dve.wait_ge(routed, 6)
            dve.tensor_reduce(top2[:], rest[:], AX.X, ALU.max).then_inc(routed, 1)
            dve.wait_ge(routed, 7)
            dve.tensor_tensor(gap[:], top2[:], top1[:], ALU.subtract).then_inc(gap_ready, 1)
            dve.tensor_tensor(hit[:], rest[:], each(top2), ALU.is_equal).then_inc(routed, 1)
            dve.wait_ge(routed, 8)
            dve.tensor_tensor(hit[:], hit[:], fall, ALU.mult).then_inc(routed, 1)
            dve.wait_ge(routed, 9)
            dve.tensor_reduce(first[:], hit[:], AX.X, ALU.max).then_inc(routed, 1)
            dve.wait_ge(routed, 10)
            dve.tensor_tensor(one2[:], fall, each(first), ALU.is_equal).then_inc(routed, 1)
            dve.wait_ge(routed, 11)
            dve.tensor_tensor(both[:], one1[:], one2[:], ALU.add).then_inc(both_ready, 1)
            dve.wait_ge(exps_done, 2)
            dve.tensor_scalar(top1[:], gap_exp[:], 1.0, None, ALU.add).then_inc(routed, 1)
            dve.tensor_scalar(top2[:], gate_exp[:], 1.0, None, ALU.add).then_inc(routed, 1)
            dve.wait_ge(routed, 13)
            dve.reciprocal(w_top[:, 0], top1[:]).then_inc(routed, 1)
            dve.reciprocal(w_shared[:], top2[:]).then_inc(routed, 1)
            dve.wait_ge(routed, 15)
            dve.tensor_tensor(w_top[:, 1], w_top[:, 0], gap_exp[:], ALU.mult).then_inc(routed, 1)
            dve.wait_ge(counted, 2)
            dve.tensor_copy(upto[0][:], ps_total[:, :, :]).then_inc(routed, 1)
            dve.wait_ge(routed, 17)
            dve.tensor_tensor(rows[:], ps_before[:, :, :], upto[0][:], ALU.subtract).then_inc(routed, 1)
            at, n, step = 0, 18, 1
            while step < TILES:
                dve.tensor_copy(upto[1 - at][:, 0:step], upto[at][:, 0:step])
                dve.tensor_tensor(upto[1 - at][:, step:], upto[at][:, step:], upto[at][:, 0:TILES - step],
                                  ALU.add).then_inc(routed, 1)
                at, n, step = 1 - at, n + 1, 2 * step
                dve.wait_ge(routed, n)
            dve.tensor_tensor(rows[:], rows[:], upto[at][:], ALU.add).then_inc(routed, 1)
            dve.tensor_copy(count_i[:], upto[at][:, TILES - 1]).then_inc(routed, 1)
            n += 2
            dve.wait_ge(routed, n)
            dve.tensor_scalar(count_i[:], count_i[:], P - 1, None, ALU.add).then_inc(routed, 1)
            dve.wait_ge(routed, n + 1)
            dve.tensor_scalar(count_i[:], count_i[:], LOG_P, None, ALU.logical_shift_right).then_inc(routed, 1)
            dve.wait_ge(routed, n + 2)
            dve.tensor_copy(room[:], count_i[:]).then_inc(routed, 1)
            dve.wait_ge(routed, n + 3)
            dve.tensor_copy(end[0][:], room[:]).then_inc(routed, 1)
            n += 4
            dve.wait_ge(routed, n)
            at, step = 0, 1
            while step < E:
                dve.tensor_copy(end[1 - at][:, 0:step], end[at][:, 0:step])
                dve.tensor_tensor(end[1 - at][:, step:], end[at][:, step:], end[at][:, 0:E - step], ALU.add).then_inc(routed, 1)
                at, n, step = 1 - at, n + 1, 2 * step
                dve.wait_ge(routed, n)
            dve.tensor_tensor(before[:], end[at][:].unsqueeze(1).broadcast_to([P, BLOCKS, E]),
                              blocks[:].unsqueeze(2).broadcast_to([P, BLOCKS, E]), ALU.is_le).then_inc(routed, 1)
            dve.tensor_tensor(room[:], end[at][:], room[:], ALU.subtract).then_inc(routed, 1)
            dve.wait_ge(routed, n + 2)
            dve.tensor_reduce(ended[:], before[:], AX.X, ALU.add).then_inc(routed, 1)
            dve.tensor_scalar(room[:], room[:], float(P), None, ALU.mult).then_inc(routed, 1)
            dve.wait_ge(routed, n + 4)
            dve.tensor_scalar(block_expert[:], ended[:], float(E - 1), None, ALU.min).then_inc(routed, 1)
            dve.tensor_tensor(rows[:], rows[:], room[:].unsqueeze(1).broadcast_to([P, TILES, E]), ALU.add).then_inc(routed, 1)
            dve.wait_ge(routed, n + 6)
            for k, one in enumerate((one1, one2)):
                dve.tensor_tensor(one[:], one[:], rows[:], ALU.mult).then_inc(routed, 1)
                dve.wait_ge(routed, n + 7 + 2 * k)
                dve.tensor_reduce((top1, top2)[k][:], one[:], AX.X, ALU.add).then_inc(routed, 1)
                dve.wait_ge(routed, n + 8 + 2 * k)
                dve.tensor_copy(pos[:, k], (top1, top2)[k][:])
            for n in range(BY_POOL, len(pieces)):
                dve.wait_ge(raw_hi, n + 1)
                dve.tensor_tensor(pieces[n][1](1), view(n), pieces[n][1](0).bitcast(F32), ALU.subtract).then_inc(raw_lo_dve, 1)


def feed_forward(nc, a, x2_all, x2T_hl, w_gu, w_dn, w_sgu, w_sdn, pos, block_expert, w_top, w_shared, xs, ys, out, ident):
    GROUP = 512
    GT = GROUP // P
    GROUPS_ALL = TILES // GT
    CHUNKS = 2 * FC
    PAIR_TILES = TILES // 2
    RING4 = 4
    BY = 8
    with ExitStack() as ctx:
        def sb(name, shape, dt=F32):
            return ctx.enter_context(nc.sbuf_tensor(name, [P] + shape, dt))

        def sem(name):
            return ctx.enter_context(nc.semaphore(name))

        xg = [sb(f"xg{p}", [2, KC, GROUP], F32R) for p in range(2)]
        hid = [sb(f"hid{p}", [GROUP]) for p in range(2)]
        hid_hl = [sb(f"hid_hl{p}", [2, GROUP], F32R) for p in range(2)]
        rows = [sb(f"rows{p}", [2, D]) for p in range(RING4)]
        where = [sb(f"where{p}", [2], I32) for p in range(RING4)]
        stats = [sb(f"f_stats{p}", [6]) for p in range(2)]
        mv = [sb(f"f_mv{p}", [2]) for p in range(2)]
        var_e = [sb(f"f_var_e{p}", [1]) for p in range(2)]
        rstd = [sb(f"f_rstd{p}", [1]) for p in range(2)]
        minus_half = sb("f_minus_half", [1])
        moved = [row[:, :, :] for row in rows]
        xe = [row[:, 0, :] for row in rows]
        ye = [row[:, 1, :] for row in rows]
        xeT_hl = [parts[:, :, 0:D].rearrange("p q (c t) -> p q c t", c=KC) for parts in hid_hl]
        heT_hl = [parts[:, :, D:D + P] for parts in hid_hl]
        he = [h[:, 0:P] for h in hid]
        ps = [ctx.enter_context(nc.psum_tensor(f"ps_f{g}", [P, 512], F32)) for g in range(8)]
        ps_gate, ps_up, ps_y = ps[0:2], ps[2:4], ps[4:8]
        ps_xeT, ps_gu, ps_heT, ps_ye = ps[0:2], ps[2:4], ps[4:6], ps[6:8]

        xg_in = [sem(f"xg_in{p}") for p in range(2)]
        gate_full = sem("gate_full")
        up_full = sem("up_full")
        silu_done = sem("silu_done")
        hid_done = sem("hid_done")
        hid_hi = sem("hid_hi")
        hid_lo = sem("hid_lo")
        y_full = sem("y_full")
        y_read = sem("y_read")
        row_copied = sem("row_copied")
        where_set = sem("where_set")
        scattered = [sem(f"scattered{p}") for p in range(RING4)]
        gathered = [sem(f"gathered{p}") for p in range(RING4)]
        xe_in = [sem(f"xe_in{p}") for p in range(RING4)]
        ye_out = [sem(f"ye_out{p}") for p in range(RING4)]
        xeT_full = sem("xeT_full")
        xeT_hi = sem("xeT_hi")
        xeT_lo = sem("xeT_lo")
        gu_full = sem("gu_full")
        he_silu = sem("he_silu")
        he_done = sem("he_done")
        heT_full = sem("heT_full")
        heT_hi = sem("heT_hi")
        heT_lo = sem("heT_lo")
        ye_full = sem("ye_full")
        ye_done = sem("ye_done")
        added = sem("added")
        summed = sem("summed")
        stats_done = sem("f_stats_done")
        mv_done = sem("f_mv_done")
        var_done = sem("f_var_done")
        rstd_done = sem("f_rstd_done")
        normed = sem("normed")
        out_done = sem("out_done")
        half_set = sem("half_set")
        met_dve = sem("h_met_dve")
        met_pool = sem("h_met_pool")

        xT_dram = x2T_hl.rearrange("q (c p) t -> p q c t", p=P)
        out_dram = out.rearrange("(t p) d -> p t d", p=P)
        xs_dram = xs.rearrange("(k p) d -> k p d", p=P)
        ys_dram = ys.rearrange("(k p) d -> k p d", p=P)

        def tile(t):
            return x2_all[:, bass.ds(t, 1), :].rearrange("p o d -> p (o d)")

        def expert_steps(eng, body, ahead=0, before=None):
            start = 3 + RING4
            turns = (BLOCKS - start) // BY - ahead

            def run(turn, steps):
                if before:
                    before(turn, steps)
                for c in steps:
                    body(Step(turn, c, BY))

            run(0, range(start))
            with eng.Fori(0, turns) as j:
                run(j, range(start, start + BY))
            run(0, range(start + BY * turns, BLOCKS + 3 + ahead))

        def there(k):
            return not k.static or 0 <= k.n < BLOCKS

        def uses(k):
            return BY // RING4 * k.turn + k.c // RING4 + 1

        block = ctx.enter_context(nc.Block())

        @block.sync
        def _(sp):
            def load_group(g, parity):
                for part in range(2):
                    sp.dma_start(xg[parity][:, part].bitcast(F32), xT_dram[:, part, :, bass.ds(g * GROUP, GROUP)]
                                 ).then_inc(xg_in[parity], 16)

            def load_pair(j):
                for parity in range(2):
                    sp.wait_ge(up_full, CHUNKS * j + FC * (parity + 1))
                    load_group(2 * j + 2 + parity, parity)

            for g in range(2):
                load_group(g, g)
            with sp.Fori(0, 2) as j:
                load_pair(j)

            for p in range(RING4):
                sp.wait_ge(scattered[p], 32 * TILES // RING4)
            def load_block(k):
                if k.least(RING4):
                    sp.wait_ge(xeT_full, k.n - RING4 + 1)
                sp.dma_start(xe[k.c % RING4][:], xs_dram[bass.ds(k.n, 1)].rearrange("o p d -> p (o d)")
                             ).then_inc(xe_in[k.c % RING4], 16)

            def step(k):
                if k.static and k.n == 0:
                    for b in range(RING4 - 1):
                        load_block(Step(0, b, BY))
                if there(k + 3):
                    load_block(k + 3)
                y = k - 4
                if there(y) and y.least(0):
                    sp.wait_ge(ye_done, y.n + 1)
                    sp.dma_start(ys_dram[bass.ds(y.n, 1)].rearrange("o p d -> p (o d)"), ye[y.c % RING4][:]
                                 ).then_inc(ye_out[y.c % RING4], 16)

            expert_steps(sp, step, 1)

            def store(t):
                sp.wait_ge(normed, t + 1)
                sp.dma_start(out_dram[:, bass.ds(t, 1), :].rearrange("p o d -> p (o d)"), tile(t)).then_inc(out_done, 16)

            load_pair(2)
            with sp.Fori(0, TILES) as t:
                store(t)
            sp.wait_ge(out_done, 16 * TILES)

        @block.tensor
        def _(pe):
            def hidden(j, c):
                g, f = c // FC, c % FC
                n = CHUNKS * j + c
                if f == 0:
                    pe.wait_ge(xg_in[g], 32 * j + 32)
                if c >= 2 or not isinstance(j, int):
                    pe.wait_ge(silu_done, n - 1)
                product(pe, ps_gate[c % 2][:, :], lambda l, k: w_sgu[:, l, k, f * P:(f + 1) * P],
                        lambda r, k: xg[g][:, r, k, :]).then_inc(gate_full, 1)
                if c >= 2 or not isinstance(j, int):
                    pe.wait_ge(hid_done, n - 1)
                product(pe, ps_up[c % 2][:, :], lambda l, k: w_sgu[:, l, k, FF_PAD + f * P:FF_PAD + (f + 1) * P],
                        lambda r, k: xg[g][:, r, k, :]).then_inc(up_full, 1)

            def down(j, c):
                g, f = c // FC, c % FC
                if f == 0 and (g > 0 or not isinstance(j, int)):
                    pe.wait_ge(y_read, GT * (2 * j + g))
                pe.wait_ge(hid_lo, CHUNKS * j + c + 1)
                for q in range(GT):
                    for n, (l, r) in enumerate(((0, 0), (1, 0), (0, 1))):
                        last = pe.matmul(ps_y[q][:, 0:D], hid_hl[c % 2][:, l, q * P:(q + 1) * P],
                                         w_sdn[:, r, f, :], start=(f == 0 and n == 0), stop=(f == FC - 1 and n == 2))
                if f == FC - 1:
                    last.then_inc(y_full, 1)

            def pair(j):
                for c in range(CHUNKS):
                    hidden(j, c)
                    if c > 0:
                        down(j, c - 1)
                down(j, CHUNKS - 1)

            pair(0)
            with pe.Fori(0, 1) as j:
                pair(j + 1)

            pe.wait_ge(hid_done, 2 * CHUNKS)
            pe.wait_ge(y_read, 2 * 2 * GT)

            expert = {}

            def load_experts(turn, steps):
                expert.clear()
                c0, c1 = max(steps[0] - 3, 0), min(steps[-1], BLOCKS)
                _, values = nc.values_load_multi_w_load_instructions(
                    block_expert[0:1, bass.ds(BY * turn + c0, c1 - c0)], engines=[mybir.EngineType.PE], min_val=0, max_val=E - 1)
                expert.update(zip(range(c0, c1), values))

            def step(k):
                b = k - 1
                if there(k):
                    pe.wait_ge(xe_in[k.c % RING4], 16 * uses(k))
                    if k.least(2):
                        pe.wait_ge(xeT_lo, k.n - 1)
                    for c in range(KC):
                        last = pe.transpose(ps_xeT[k.c % 2][:, c * P:(c + 1) * P], xe[k.c % RING4][:, c * P:(c + 1) * P], ident[:, :])
                    last.then_inc(xeT_full, 1)
                if b.least(0) and there(b):
                    e = expert[b.c]
                    pe.wait_ge(xeT_lo, b.n + 1)
                    if b.least(2):
                        pe.wait_ge(he_done, b.n - 1)
                    product(pe, ps_gu[b.c % 2][:, 0:D], lambda l, c: xeT_hl[b.c % 2][:, l, c, :],
                            lambda r, c: w_gu[:, bass.ds(e, 1), r, c, :].rearrange("p o n -> p (o n)")).then_inc(gu_full, 1)
                b = k - 2
                if b.least(0) and there(b):
                    pe.wait_ge(he_done, b.n + 1)
                    if b.least(2):
                        pe.wait_ge(heT_lo, b.n - 1)
                    pe.transpose(ps_heT[b.c % 2][:, 0:P], he[b.c % 2][:, :], ident[:, :]).then_inc(heT_full, 1)
                b = k - 3
                if b.least(0) and there(b):
                    e = expert[b.c]
                    pe.wait_ge(heT_lo, b.n + 1)
                    if b.least(2):
                        pe.wait_ge(ye_done, b.n - 1)
                    product(pe, ps_ye[b.c % 2][:, 0:D], lambda l, c: heT_hl[b.c % 2][:, l, :],
                            lambda r, c: w_dn[:, bass.ds(e, 1), r, :].rearrange("p o n -> p (o n)"), 1).then_inc(ye_full, 1)

            expert_steps(pe, step, before=load_experts)

            pe.wait_ge(heT_lo, BLOCKS)
            pe.wait_ge(ye_done, BLOCKS)
            with pe.Fori(0, 2) as j:
                pair(j + 2)

        @block.scalar
        def _(act):
            def chunk(j, c):
                n = CHUNKS * j + c
                act.wait_ge(gate_full, n + 1)
                if c >= 2 or not isinstance(j, int):
                    act.wait_ge(hid_lo, n - 1)
                act.activation(hid[c % 2][:], ps_gate[c % 2][:, :], ACT.Silu).then_inc(silu_done, 1)
                act.wait_ge(hid_done, n + 1)
                if c >= 2 or not isinstance(j, int):
                    act.wait_ge(up_full, n)
                act.copy(hid_hl[c % 2][:, 0], hid[c % 2][:]).then_inc(hid_hi, 1)

            def pair(j):
                for c in range(CHUNKS):
                    chunk(j, c)

            pair(0)
            with act.Fori(0, 1) as j:
                pair(j + 1)

            def step(k):
                if there(k):
                    act.wait_ge(xeT_full, k.n + 1)
                    if k.least(2):
                        act.wait_ge(gu_full, k.n - 1)
                    act.copy(xeT_hl[k.c % 2][:, 0], ps_xeT[k.c % 2][:, 0:D].rearrange("p (c t) -> p c t", c=KC)).then_inc(xeT_hi, 1)
                b = k - 1
                if b.least(0) and there(b):
                    act.wait_ge(gu_full, b.n + 1)
                    if b.least(2):
                        act.wait_ge(heT_full, b.n - 1)
                    act.activation(he[b.c % 2][:], ps_gu[b.c % 2][:, 0:P], ACT.Silu).then_inc(he_silu, 1)
                b = k - 2
                if b.least(0) and there(b):
                    act.wait_ge(heT_full, b.n + 1)
                    if b.least(2):
                        act.wait_ge(ye_full, b.n - 1)
                    act.copy(heT_hl[b.c % 2][:, 0], ps_heT[b.c % 2][:, 0:P]).then_inc(heT_hi, 1)

            expert_steps(act, step)
            with act.Fori(0, 2) as j:
                pair(j + 2)

        @block.vector
        def _(dve):
            def chunk(j, c):
                n = CHUNKS * j + c
                dve.wait_ge(silu_done, n + 1)
                dve.wait_ge(up_full, n + 1)
                dve.tensor_tensor(hid[c % 2][:], hid[c % 2][:], ps_up[c % 2][:, :], ALU.mult).then_inc(hid_done, 1)
                dve.wait_ge(hid_hi, n + 1)
                dve.tensor_tensor(hid_hl[c % 2][:, 1], hid[c % 2][:], hid_hl[c % 2][:, 0].bitcast(F32), ALU.subtract).then_inc(hid_lo, 1)

            def outputs(j, g):
                dve.wait_ge(y_full, 2 * j + g + 1)
                dve.wait_ge(row_copied, GT * (2 * j + g + 1))
                for q in range(GT):
                    t = GT * (2 * j + g) + q
                    dve.scalar_tensor_tensor(out=tile(t), in0=ps_y[q][:, 0:D],
                                             scalar=w_shared[:, bass.ds(t, 1)], in1=tile(t), op0=ALU.mult,
                                             op1=ALU.add).then_inc(y_read, 1)

            def combine(j, c):
                t = PAIR_TILES * j + c
                v = tile(t)
                dve.wait_ge(gathered[c % RING4], 32 * (PAIR_TILES // RING4 * j + c // RING4) + 32)
                dve.scalar_tensor_tensor(out=v, in0=moved[c % RING4][:, 0], scalar=w_top[:, 0, bass.ds(t, 1)], in1=v, op0=ALU.mult,
                                         op1=ALU.add).then_inc(added, 1)
                dve.wait_ge(added, t + 1)
                dve.scalar_tensor_tensor(out=v, in0=moved[c % RING4][:, 1], scalar=w_top[:, 1, bass.ds(t, 1)], in1=v, op0=ALU.mult,
                                         op1=ALU.add).then_inc(summed, 1)
                dve.wait_ge(summed, t + 1)
                apart(dve, met_dve)
                dve.bn_stats(stats[c % 2][:], v).then_inc(stats_done, 1)
                dve.wait_ge(stats_done, t + 1)
                apart(dve, met_dve)
                dve.bn_aggr(mv[c % 2][:], stats[c % 2][:]).then_inc(mv_done, 1)

            def norm(j, c):
                t = PAIR_TILES * j + c
                dve.wait_ge(mv_done, t + 1)
                dve.wait_ge(rstd_done, t + 1)
                dve.tensor_scalar(tile(t), tile(t), mv[c % 2][:, 0:1], rstd[c % 2][:], ALU.subtract, ALU.mult).then_inc(normed, 1)

            def pair(j, finish=None):
                for c in range(CHUNKS):
                    chunk(j, c)
                    if c == FC:
                        outputs(j, 0)
                        if finish is not None:
                            dve.wait_ge(y_read, GT * (2 * j + 1))
                    if finish is not None:
                        combine(finish, c)
                        if c > 0:
                            norm(finish, c - 1)
                outputs(j, 1)
                if finish is not None:
                    dve.wait_ge(y_read, GT * (2 * j + 2))
                    for c in range(CHUNKS, PAIR_TILES):
                        combine(finish, c)
                        norm(finish, c - 1)
                    norm(finish, PAIR_TILES - 1)

            pair(0)
            with dve.Fori(0, 1) as j:
                pair(j + 1)

            def step(k):
                if there(k):
                    dve.wait_ge(xeT_hi, k.n + 1)
                    dve.tensor_tensor(xeT_hl[k.c % 2][:, 1], ps_xeT[k.c % 2][:, 0:D].rearrange("p (c t) -> p c t", c=KC),
                                      xeT_hl[k.c % 2][:, 0].bitcast(F32), ALU.subtract).then_inc(xeT_lo, 1)
                b = k - 1
                if b.least(0) and there(b):
                    dve.wait_ge(he_silu, b.n + 1)
                    dve.tensor_tensor(he[b.c % 2][:], he[b.c % 2][:], ps_gu[b.c % 2][:, P:2 * P], ALU.mult).then_inc(he_done, 1)
                b = k - 2
                if b.least(0) and there(b):
                    dve.wait_ge(heT_hi, b.n + 1)
                    dve.tensor_tensor(heT_hl[b.c % 2][:, 1], ps_heT[b.c % 2][:, 0:P], heT_hl[b.c % 2][:, 0].bitcast(F32),
                                      ALU.subtract).then_inc(heT_lo, 1)
                b = k - 3
                if b.least(0) and there(b):
                    dve.wait_ge(ye_full, b.n + 1)
                    if b.least(RING4):
                        dve.wait_ge(ye_out[b.c % RING4], 16 * uses(b) - 16)
                    dve.tensor_copy(ye[b.c % RING4][:], ps_ye[b.c % 2][:, 0:D]).then_inc(ye_done, 1)

            expert_steps(dve, step)
            with dve.Fori(0, 2) as j:
                pair(j + 2, j)

        @block.gpsimd
        def _(pool):
            pool.memset(minus_half[:], -0.5).then_inc(half_set, 1)
            pool.wait_ge(half_set, 1)

            def scatter(j, c):
                t = RING4 * j + c
                if not isinstance(j, int):
                    pool.wait_ge(scattered[c], 32 * j)
                apart(pool, met_pool)
                pool.tensor_copy(where[c][:], pos[:, :, bass.ds(t, 1)].rearrange("p k o -> p (k o)")).then_inc(where_set, 1)
                pool.tensor_copy(moved[c][:, 0], tile(t)).then_inc(row_copied, 1)
                pool.wait_ge(where_set, t + 1)
                pool.wait_ge(row_copied, t + 1)
                apart(pool, met_pool)
                for k in range(2):
                    pool.indirect_dma_start(out=xs, out_offset=bass.IndirectOffsetOnAxis(ap=where[c][:, k:k + 1], axis=0),
                                            in_=moved[c][:, 0], in_offset=None).then_inc(scattered[c], 16)

            for c in range(RING4):
                scatter(0, c)
            with pool.Fori(0, TILES // RING4 - 1) as j:
                for c in range(RING4):
                    scatter(j + 1, c)

            for p in range(RING4):
                pool.wait_ge(ye_out[p], 16 * ((BLOCKS - p + RING4 - 1) // RING4))

            def gather(j, c):
                t = RING4 * j + c
                if not isinstance(j, int):
                    pool.wait_ge(summed, t - RING4 + 1)
                apart(pool, met_pool)
                pool.tensor_copy(where[c][:], pos[:, :, bass.ds(t, 1)].rearrange("p k o -> p (k o)")).then_inc(where_set, 1)
                pool.wait_ge(where_set, TILES + t + 1)
                apart(pool, met_pool)
                for k in range(2):
                    pool.indirect_dma_start(out=moved[c][:, k], out_offset=None, in_=ys,
                                            in_offset=bass.IndirectOffsetOnAxis(ap=where[c][:, k:k + 1], axis=0)
                                            ).then_inc(gathered[c], 16)

            def root(j, c):
                t = RING4 * j + c
                pool.wait_ge(mv_done, t + 1)
                apart(pool, met_pool)
                pool.tensor_scalar(var_e[c % 2][:], mv[c % 2][:, 1:2], EPS, None, ALU.add).then_inc(var_done, 1)
                pool.wait_ge(var_done, t + 1)
                pool.tensor_tensor(rstd[c % 2][:], var_e[c % 2][:], minus_half[:], ALU.pow).then_inc(rstd_done, 1)

            for c in range(RING4):
                gather(0, c)
            with pool.Fori(0, TILES // RING4 - 1) as j:
                for c in range(RING4):
                    root(j, c)
                    gather(j + 1, c)
            for c in range(RING4):
                root(TILES // RING4 - 1, c)


def layer(nc, a, out):
    def dram(name, shape):
        return nc.dram_tensor(name, shape, F32, kind="Internal").ap()

    stacks = dram("stacks", (2, 2, 2, D, N))
    heads = dram("heads_out", (H * 2 * HD, NB * N))
    x2T_hl = dram("x2T_parts", (2, D, NB * N))
    xs = dram("expert_rows", (CLEAR * NB * P, D))
    ys = dram("expert_outputs", (BLOCKS * P, D))
    with ExitStack() as ctx:
        def sb(name, shape, dt=F32):
            return ctx.enter_context(nc.sbuf_tensor(name, [P] + shape, dt))

        ident = sb("ident", [P])
        self_attention(nc, a, heads, stacks, ident, xs)
        logits = sb("logits", [TILES, NR])
        x2_all = sb("x2_all", [TILES, D])
        cross_attention(nc, a, heads, x2_all, x2T_hl, logits, ident)
        w_gu = sb("w_gu", [E, 2, KC, 2 * P], F32R)
        w_dn = sb("w_dn", [E, 2, D], F32R)
        w_sgu = sb("w_sgu", [2, KC, 2 * FF_PAD], F32R)
        w_sdn = sb("w_sdn", [2, FC, D], F32R)
        pos = sb("pos", [2, TILES], I32)
        block_expert = sb("block_expert", [BLOCKS], I32)
        w_top = sb("w_top", [2, TILES])
        w_shared = sb("w_shared", [TILES])
        routing(nc, a, logits, w_gu, w_dn, w_sgu, w_sdn, pos, block_expert, w_top, w_shared)
        feed_forward(nc, a, x2_all, x2T_hl, w_gu, w_dn, w_sgu, w_sdn, pos, block_expert, w_top, w_shared, xs, ys, out, ident)


def host_arrays(v):
    f = {k: np.ascontiguousarray(x) for k, x in v.items()}
    out = {
        "x": f["x"],
        "xT": np.ascontiguousarray(f["x"].reshape(NB * N, D).T),
        "ctxT": np.ascontiguousarray(f["ctx_1024"].reshape(NB * N, D).T),
        "qkvT": np.ascontiguousarray(f["L0_attn_qkv_w"].T),
        "qkv_b": f["L0_attn_qkv_b"],
        "projT": np.ascontiguousarray(f["L0_attn_proj_w"].T.reshape(HD, HD, D).transpose(1, 0, 2).reshape(D, D)),
        "proj_b": f["L0_attn_proj_b"],
        "WqT": np.ascontiguousarray(f["L0_xattn_Wq"].T),
        "WkT": np.ascontiguousarray(f["L0_xattn_Wk"].T),
        "WvT": np.ascontiguousarray(f["L0_xattn_Wv"].T),
        "bq2": np.ascontiguousarray(f["L0_xattn_bq"].reshape(KC, P).T),
        "bk2": np.ascontiguousarray(f["L0_xattn_bk"].reshape(KC, P).T),
        "bv": f["L0_xattn_bv"],
        "routerT": np.ascontiguousarray(np.concatenate(
            [f["L0_ffn_gate_w"], f["L0_ffn_shared_gate_w"], np.zeros((P - E - 1, D), np.float32)]).T),
    }
    inv = (1.0 / np.float32(10000.0) ** (np.arange(0, HD, 2, dtype=np.float32) / np.float32(HD))).astype(np.float32)
    angle = np.arange(N, dtype=np.float32)[:, None] * inv[None, :]
    angle = np.concatenate([angle, angle], axis=1)
    sign = np.where(np.arange(HD) < HD // 2, -1.0, 1.0).astype(np.float32)
    scale = np.array([HD ** -0.5, 1.0], np.float32)[None, :, None]
    out["cos"] = np.ascontiguousarray(np.cos(angle)[:, None, :] * scale)
    out["sin"] = np.ascontiguousarray((np.sin(angle) * sign)[:, None, :] * scale)
    out["shared_guT"] = np.zeros((D, 2, FF_PAD), np.float32)
    out["shared_guT"][:, 0, :FF] = f["L0_ffn_shared_w_gate"].T
    out["shared_guT"][:, 1, :FF] = f["L0_ffn_shared_w_up"].T
    out["shared_guT"] = out["shared_guT"].reshape(D, 2 * FF_PAD)
    out["shared_dnT"] = np.zeros((FF_PAD, D), np.float32)
    out["shared_dnT"][:FF] = f["L0_ffn_shared_w_down"].T
    out["w_gate_up"] = f["L0_ffn_w_gate_up"]
    out["w_down"] = f["L0_ffn_w_down"]
    out["tri"] = np.triu(np.ones((P, P), np.float32), 1)
    out["falling"] = np.tile(np.arange(E, 0, -1, dtype=np.float32), (P, 1))
    out["blocks"] = np.tile(np.arange(BLOCKS, dtype=np.float32), (P, 1))
    out["ident"] = np.eye(P, dtype=np.float32)
    return out


def kernel(**inputs):
    import concourse.bacc as bacc
    from concourse.bass_utils import run_bass_kernel_spmd

    nc = bacc.Bacc("TRN2", target_bir_lowering=False, num_devices=1)
    arrays = {f"in_{k}": v for k, v in host_arrays(inputs).items()}
    a = {k[3:]: nc.dram_tensor(k, v.shape, mybir.dt.from_np(v.dtype), kind="ExternalInput").ap() for k, v in arrays.items()}
    out = nc.dram_tensor("out", (NB, N, D), F32, kind="ExternalOutput").ap()
    layer(nc, a, out.rearrange("b t d -> (b t) d"))
    return run_bass_kernel_spmd(nc, [arrays], core_ids=[0]).results[0]["out"]
```
